# Optimizing a Trainium2 kernel written in Bass

```python
import numpy as np
import jax
import jax.numpy as jnp

def _softmax(x, axis=-1):
    return jax.nn.softmax(x, axis=axis)

def _gelu(x):
    return jax.nn.gelu(x, approximate=True)

def _silu(x):
    return jax.nn.silu(x)

def _sigmoid(x):
    return jax.nn.sigmoid(x)

def _layernorm(x, axis=-1, eps=1e-05):
    m = jnp.mean(x, axis=axis, keepdims=True)
    v = jnp.var(x, axis=axis, keepdims=True)
    return (x - m) / jnp.sqrt(v + eps)

def _scatter_add(tgt, idx, src, axis=0):
    return tgt.at[idx].add(src)

def _segment_sum(src, seg, n):
    return jax.ops.segment_sum(src, seg, n)
kernel_name = 'mk_seq_postln_d1_jaxref_r4_3487b8'

def setup_inputs(seed: int=0):
    np.random.seed(seed)
    _w = jnp.asarray

    def _L0_attn_setup():
        import jax, jax.numpy as jnp
        import numpy as np
        N_HEAD = 16
        LATENT = 32

        def _rotate_half(x):
            xe = x[..., ::2]
            xo = x[..., 1::2]
            return jnp.stack((-xo, xe), axis=-1).reshape(x.shape)

        def _rope_tables(T, latent_dim, dtype):
            inv_freq = 1.0 / 10000.0 ** (jnp.arange(0, latent_dim, 2, dtype=jnp.float32) / latent_dim)
            t = jnp.arange(T, dtype=jnp.float32)
            freqs = jnp.outer(t, inv_freq)
            cos = jnp.repeat(jnp.cos(freqs), 2, axis=-1)[:, :latent_dim]
            sin = jnp.repeat(jnp.sin(freqs), 2, axis=-1)[:, :latent_dim]
            return (cos.astype(dtype), sin.astype(dtype))
        key = jax.random.key(seed)
        ks = jax.random.split(key, 14)
        C = 256
        hd = C // N_HEAD
        L = LATENT
        s = 0.02
        return {'x': jax.random.normal(ks[0], (4, 512, C), jnp.float32), 'c_attn_w': jax.random.normal(ks[1], (3 * C, C), jnp.float32) * s, 'c_attn_b': jnp.zeros((3 * C,), jnp.float32), 'q2l_w': jax.random.normal(ks[2], (L, hd), jnp.float32) * s, 'q2l_b': jnp.zeros((L,), jnp.float32), 'kv2l_w': jax.random.normal(ks[3], (L, hd), jnp.float32) * s, 'kv2l_b': jnp.zeros((L,), jnp.float32), 'l2o_w': jax.random.normal(ks[4], (hd, L), jnp.float32) * s, 'l2o_b': jnp.zeros((hd,), jnp.float32), 'wqk_w': jax.random.normal(ks[5], (L, L), jnp.float32) * s, 'wqk_b': jnp.zeros((L,), jnp.float32), 'cproj_w': jax.random.normal(ks[6], (C, C), jnp.float32) * s, 'cproj_b': jnp.zeros((C,), jnp.float32)}
    _L0_attn_in = _L0_attn_setup()

    def _L0_ffn_setup():
        import jax, jax.numpy as jnp
        import numpy as np
        B, N, D = (4, 1024, 256)
        E, S, F = (16, 64, 512)
        DO = 256
        EPS = 1e-05

        def _layernorm(x, g, b):
            mu = jnp.mean(x, axis=-1, keepdims=True)
            var = jnp.mean(jnp.square(x - mu), axis=-1, keepdims=True)
            return (x - mu) * jax.lax.rsqrt(var + EPS) * g + b
        key = jax.random.key(seed)
        ks = jax.random.split(key, 8)
        d = {'x': jax.random.normal(ks[0], (B, N, D), dtype=jnp.float32), 'norm_g': jnp.ones((D,), jnp.float32), 'norm_b': jnp.zeros((D,), jnp.float32), 'slot_g': jnp.ones((D,), jnp.float32), 'slot_b': jnp.zeros((D,), jnp.float32), 'scale': jnp.ones((1,), jnp.float32), 'slot_embeds': jax.random.normal(ks[1], (E, S, D), jnp.float32) / np.sqrt(D), 'Wg': jax.random.normal(ks[2], (E, D, F), jnp.float32) * np.sqrt(2.0 / (D + F)), 'bg': jnp.zeros((E, F), jnp.float32), 'Wu': jax.random.normal(ks[3], (E, D, F), jnp.float32) * np.sqrt(2.0 / (D + F)), 'bu': jnp.zeros((E, F), jnp.float32), 'Wd': jax.random.normal(ks[4], (E, F, DO), jnp.float32) * np.sqrt(2.0 / (F + DO)), 'bd': jnp.zeros((E, DO), jnp.float32)}
        return d
    _L0_ffn_in = _L0_ffn_setup()
    _d = {'L0_attn_x': _L0_attn_in['x'], 'L0_attn_c_attn_w': _L0_attn_in['c_attn_w'], 'L0_attn_c_attn_b': _L0_attn_in['c_attn_b'], 'L0_attn_q2l_w': _L0_attn_in['q2l_w'], 'L0_attn_q2l_b': _L0_attn_in['q2l_b'], 'L0_attn_kv2l_w': _L0_attn_in['kv2l_w'], 'L0_attn_kv2l_b': _L0_attn_in['kv2l_b'], 'L0_attn_l2o_w': _L0_attn_in['l2o_w'], 'L0_attn_l2o_b': _L0_attn_in['l2o_b'], 'L0_attn_wqk_w': _L0_attn_in['wqk_w'], 'L0_attn_wqk_b': _L0_attn_in['wqk_b'], 'L0_attn_cproj_w': _L0_attn_in['cproj_w'], 'L0_attn_cproj_b': _L0_attn_in['cproj_b'], 'L0_ffn_norm_g': _L0_ffn_in['norm_g'], 'L0_ffn_norm_b': _L0_ffn_in['norm_b'], 'L0_ffn_slot_g': _L0_ffn_in['slot_g'], 'L0_ffn_slot_b': _L0_ffn_in['slot_b'], 'L0_ffn_scale': _L0_ffn_in['scale'], 'L0_ffn_slot_embeds': _L0_ffn_in['slot_embeds'], 'L0_ffn_Wg': _L0_ffn_in['Wg'], 'L0_ffn_bg': _L0_ffn_in['bg'], 'L0_ffn_Wu': _L0_ffn_in['Wu'], 'L0_ffn_bu': _L0_ffn_in['bu'], 'L0_ffn_Wd': _L0_ffn_in['Wd'], 'L0_ffn_bd': _L0_ffn_in['bd']}
    _x0 = _d['L0_attn_x']
    _d['L0_attn_x'] = jax.random.normal(jax.random.fold_in(jax.random.key(seed), 1), (8, 512, 256), dtype=_x0.dtype)
    del _x0
    return _d

def reference(L0_attn_x, L0_attn_c_attn_w, L0_attn_c_attn_b, L0_attn_q2l_w, L0_attn_q2l_b, L0_attn_kv2l_w, L0_attn_kv2l_b, L0_attn_l2o_w, L0_attn_l2o_b, L0_attn_wqk_w, L0_attn_wqk_b, L0_attn_cproj_w, L0_attn_cproj_b, L0_ffn_norm_g, L0_ffn_norm_b, L0_ffn_slot_g, L0_ffn_slot_b, L0_ffn_scale, L0_ffn_slot_embeds, L0_ffn_Wg, L0_ffn_bg, L0_ffn_Wu, L0_ffn_bu, L0_ffn_Wd, L0_ffn_bd):

    def _L0_attn_ref(x, c_attn_w, c_attn_b, q2l_w, q2l_b, kv2l_w, kv2l_b, l2o_w, l2o_b, wqk_w, wqk_b, cproj_w, cproj_b):
        import jax, jax.numpy as jnp
        import numpy as np
        N_HEAD = 16
        LATENT = 32

        def _rotate_half(x):
            xe = x[..., ::2]
            xo = x[..., 1::2]
            return jnp.stack((-xo, xe), axis=-1).reshape(x.shape)

        def _rope_tables(T, latent_dim, dtype):
            inv_freq = 1.0 / 10000.0 ** (jnp.arange(0, latent_dim, 2, dtype=jnp.float32) / latent_dim)
            t = jnp.arange(T, dtype=jnp.float32)
            freqs = jnp.outer(t, inv_freq)
            cos = jnp.repeat(jnp.cos(freqs), 2, axis=-1)[:, :latent_dim]
            sin = jnp.repeat(jnp.sin(freqs), 2, axis=-1)[:, :latent_dim]
            return (cos.astype(dtype), sin.astype(dtype))
        B, T, C = x.shape
        H = N_HEAD
        hd = C // H
        L = q2l_w.shape[0]
        qkv = x @ c_attn_w.T + c_attn_b
        q, k, v = jnp.split(qkv, 3, axis=2)

        def heads(t):
            return t.reshape(B, T, H, hd).transpose(0, 2, 1, 3)
        q, k, v = (heads(q), heads(k), heads(v))
        q_lat = q @ q2l_w.T + q2l_b
        k_lat = k @ kv2l_w.T + kv2l_b
        v_lat = v @ kv2l_w.T + kv2l_b
        cos, sin = _rope_tables(T, L, x.dtype)
        cos = cos[None, None]
        sin = sin[None, None]
        q_lat = q_lat * cos + _rotate_half(q_lat) * sin
        k_lat = k_lat * cos + _rotate_half(k_lat) * sin
        q_for_k = q_lat @ wqk_w.T + wqk_b
        att = jnp.einsum('bhql,bhkl->bhqk', q_for_k, k_lat) * L ** (-0.5)
        causal = jnp.tril(jnp.ones((T, T), dtype=bool))
        att = jnp.where(causal[None, None], att, -jnp.inf)
        att = jax.nn.softmax(att, axis=-1)
        y_lat = jnp.einsum('bhqk,bhkl->bhql', att, v_lat)
        y = y_lat @ l2o_w.T + l2o_b
        y = y.transpose(0, 2, 1, 3).reshape(B, T, C)
        return y @ cproj_w.T + cproj_b

    def _L0_ffn_ref(x, norm_g, norm_b, slot_g, slot_b, scale, slot_embeds, Wg, bg, Wu, bu, Wd, bd):
        import jax, jax.numpy as jnp
        import numpy as np
        B, N, D = (4, 1024, 256)
        E, S, F = (16, 64, 512)
        DO = 256
        EPS = 1e-05

        def _layernorm(x, g, b):
            mu = jnp.mean(x, axis=-1, keepdims=True)
            var = jnp.mean(jnp.square(x - mu), axis=-1, keepdims=True)
            return (x - mu) * jax.lax.rsqrt(var + EPS) * g + b
        x = _layernorm(x, norm_g, norm_b)
        se = _layernorm(slot_embeds, slot_g, slot_b) * scale
        logits = jnp.einsum('bnd,esd->bnes', x, se)
        dispatch = jax.nn.softmax(logits, axis=1)
        combine = jax.nn.softmax(logits.reshape(x.shape[0], x.shape[1], -1), axis=-1)
        slots = jnp.einsum('bnd,bnes->besd', x, dispatch)
        gate = jax.nn.gelu(jnp.einsum('besd,edf->besf', slots, Wg) + bg[None, :, None, :], approximate=False)
        up = jnp.einsum('besd,edf->besf', slots, Wu) + bu[None, :, None, :]
        eout = jnp.einsum('besf,efo->beso', gate * up, Wd) + bd[None, :, None, :]
        eout = eout.reshape(eout.shape[0], -1, eout.shape[-1])
        return jnp.einsum('bns,bso->bno', combine, eout)
    x = L0_attn_x
    x = _layernorm(x + _L0_attn_ref(x, L0_attn_c_attn_w, L0_attn_c_attn_b, L0_attn_q2l_w, L0_attn_q2l_b, L0_attn_kv2l_w, L0_attn_kv2l_b, L0_attn_l2o_w, L0_attn_l2o_b, L0_attn_wqk_w, L0_attn_wqk_b, L0_attn_cproj_w, L0_attn_cproj_b), axis=-1)
    x = _layernorm(x + _L0_ffn_ref(x, L0_ffn_norm_g, L0_ffn_norm_b, L0_ffn_slot_g, L0_ffn_slot_b, L0_ffn_scale, L0_ffn_slot_embeds, L0_ffn_Wg, L0_ffn_bg, L0_ffn_Wu, L0_ffn_bu, L0_ffn_Wd, L0_ffn_bd), axis=-1)
    return x

_drawn_inputs = setup_inputs


def setup_inputs(seed=0):
    import zlib

    import numpy as np

    out = dict(_drawn_inputs(seed))
    spreads = {'L0_attn_c_attn_b': (0.0, 0.8),
     'L0_attn_q2l_b': (0.0, 0.8),
     'L0_attn_kv2l_b': (0.0, 0.8),
     'L0_attn_l2o_b': (0.0, 0.1),
     'L0_attn_wqk_b': (0.0, 0.8),
     'L0_attn_cproj_b': (0.0, 0.1),
     'L0_ffn_norm_g': (1.0, 0.2),
     'L0_ffn_norm_b': (0.0, 0.1),
     'L0_ffn_slot_g': (1.0, 0.2),
     'L0_ffn_slot_b': (0.0, 0.1),
     'L0_ffn_bg': (0.0, 0.1),
     'L0_ffn_bu': (0.0, 0.1),
     'L0_ffn_bd': (0.0, 0.1)}
    factors = {'L0_attn_c_attn_w': 8.0,
     'L0_attn_q2l_w': 8.0,
     'L0_attn_kv2l_w': 8.0,
     'L0_attn_l2o_w': 8.0,
     'L0_attn_wqk_w': 8.0}
    for name, (base, spread) in spreads.items():
        noise = np.random.default_rng([zlib.crc32(name.encode()), seed]).standard_normal(out[name].shape)
        drawn = base * np.exp(spread * noise) if base else spread * noise
        out[name] = jnp.asarray(drawn.astype(out[name].dtype))
    for name, factor in factors.items():
        out[name] = (out[name] * factor).astype(out[name].dtype)
    return out
```

```python
import concourse.bass as bass
from concourse import mybir


B, T, C = 8, 512, 256
H, HD, L = 16, 16, 32
E, S, F, DO = 16, 64, 512, 256
P = 128
GH = P // L
G = H // GH
NT = T // P
NC = C // P
NS = E * S // P
NF = F // P
NP = E // 2
TERMS = 3
KS_ROWS = TERMS * L
EPS = 1e-5
SCALE = float(L) ** -0.5
MASKED = -1e30
RSQRT_MAGIC = 1597463007.0
NEWTON = 3
RING = 3
ST_LAG = 13


def batch_schedule():
    steps = [("xT",), ("qk", 0), ("qk", 1), ("v",), ("latent", 0), ("latent", 1), ("wqk", 0), ("wqk", 1)]
    units = 2 * NT * G
    for u in range(units + ST_LAG + 6):
        if u in (2, 10):
            steps.append(("latent", u // 8 + 2))
        if u in (7, 15):
            steps.append(("wqk", u // 8 + 2))
        if u < units:
            steps.append(("max", u // 8, u % 8 // 2, u % 2))
        if u >= 9 and (u - 9) % 8 == 0 and (u - 9) // 8 < G:
            steps.append(("negmax", (u - 9) // 8))
        v = u - ST_LAG
        if 0 <= v < units:
            steps.append(("exp", v // 8, v % 8 // 2, v % 2))
        w = v - 2
        if w >= 0 and w % 2 == 1 and w < units:
            steps.append(("pv", w // 8, w % 8 // 2))
            if w % 8 == 7:
                steps.append(("y", w // 8))
        if v - 5 >= 0 and (v - 5) % 8 == 7 and (v - 5) // 8 < G:
            steps.append(("ynorm", (v - 5) // 8))
    steps += [("ynorm", G - 1)] if ("ynorm", G - 1) not in steps else []
    steps += [("cproj",), ("zT",), ("s1", 0), ("s1", 1), ("c1norm", 0), ("s1", 2), ("c1norm", 1), ("s1", 3),
              ("c1norm", 2), ("s2", 0), ("c1norm", 3), ("s2", 1), ("e2norm", 0), ("c2", 0), ("d", 0),
              ("e2norm", 1), ("s2", 2), ("d", 1), ("c2", 1), ("slots", 0), ("e2norm", 2), ("s2", 3), ("d", 2),
              ("e2norm", 3), ("c2", 2), ("d", 3), ("c2", 3), ("slots", 1)]
    return steps


PAIR_STEPS = ("xT", "qk", "v", "latent", "max", "exp", "cproj", "zT", "s1", "s2", "d", "c2", "slots")
MISC_STEPS = ("wqk", "negmax", "ynorm")


def block_kernel(nc, a, out):
    f32, f32r, bf16, i32 = mybir.dt.float32, mybir.dt.float32r, mybir.dt.bfloat16, mybir.dt.int32
    ALU, ACT, AX = mybir.AluOpType, mybir.ActivationFunctionType, mybir.AxisListType

    steps = batch_schedule()
    pair_no = {s: n for n, s in enumerate(s for s in steps if s[0] in PAIR_STEPS)}
    misc_no = {s: n for n, s in enumerate(s for s in steps if s[0] in MISC_STEPS)}
    PAIRS = len(pair_no)
    FILLS = [len(range(r, PAIRS, RING)) for r in range(RING)]

    x1_dram = nc.dram_tensor("x1_dram", (B, P, NT * C), f32).ap()
    c2_dram = nc.dram_tensor("c2_dram", (B, P, NS * T), f32).ap()
    sl_dram = nc.dram_tensor("sl_dram", (E, P, NC, B, S), f32).ap()

    KB = 1024
    at = [(nc.sbuf_base + 63) // 64 * 64]

    def place(name, shape, dt, offset=None):
        size = 2 if dt == bf16 else 4
        for n in shape[1:]:
            size *= n
        size = (size + 31) // 32 * 32
        base = at[0] if offset is None else offset
        if offset is None:
            at[0] += size
        assert base + size <= nc.sbuf_usable_end, (name, base + size)
        return nc.alloc_sbuf_tensor_at(name, shape, dt, offset=base)

    ident = place("ident", [P, P], f32)
    const_end = at[0]
    identb = place("identb", [P, P], bf16)
    maskb = place("maskb", [P, P], bf16)
    w3h = place("w3h", [P, NC, 3 * C], f32r)
    w3l = place("w3l", [P, NC, 3 * C], f32r)
    wlh = place("wlh", [P, 2, P], f32r)
    wll = place("wll", [P, 2, P], f32r)
    wq = place("wq", [P, P], f32)
    cw = place("cw", [P, G, C], f32)
    seh = place("seh", [P, NC, E * S], f32r)
    sel_ = place("sel_", [P, NC, E * S], f32r)
    cos = place("cos", [P, T], f32)
    sin = place("sin", [P, T], f32)
    pick = place("pick", [P, P], f32)
    bqk = place("bqk", [P, 4], f32)
    blat = place("blat", [P, 2], f32)
    bwq = place("bwq", [P, 1], f32)
    ng = place("ng", [P, NC], f32)
    nb_ = place("nb_", [P, NC], f32)
    bv = place("bv", [P, C], f32)
    negmax = place("negmax", [P, G, NT, GH, 2], f32)
    mx = place("mx", [P, G, NT, GH], f32)
    small = place("small", [P, 64], f32)
    M1, CS, RCS = small[:, 0:4], small[:, 4:8], small[:, 8:12]
    M2, ES, RES = small[:, 12:20], small[:, 20:28], small[:, 28:36]
    stats = place("stats", [P, 8, 6], f32)
    meanvar = place("meanvar", [P, 8, 2], f32)
    nv, ny, nt_ = (place(n, [P, 8], f32) for n in ("nv", "ny", "nt_"))
    x = place("x", [P, NT, C], f32)
    va = place("va", [P, NT, H, L], f32)
    stg = [place(f"stg{i}", [P, 4, T], f32r) for i in range(2)]
    pt = [place(f"pt{i}", [P, GH, T], f32) for i in range(2)]
    ones2 = place("ones2", [2, T], f32)
    ys = place("ys", [P, T], f32)
    rc = place("rc", [P, T], f32)
    yn = place("yn", [P, G, T], f32)
    mts = [place(f"mts{i}", [2 * GH, T], f32r) for i in range(2)]
    r0 = at[0]
    qks = place("qks", [P, G, GH, 2, T], f32r)
    r1 = at[0]
    qth = place("qth", [P, 4, T], f32r)
    qtl = place("qtl", [P, 4, T], f32r)
    r2 = at[0]
    xth = place("xth", [P, NC, T], f32r)
    xtl = place("xtl", [P, NC, T], f32r)
    r3 = at[0]
    lat = place("lat", [P, 2, T], f32)
    rot = place("rot", [P, 2, T], f32)
    rope = place("rope", [P, 2, T], f32)
    c1 = place("c1", [P, NT, E * S], f32, r0)
    e2 = [place(f"e2{i}", [P, 2, T], f32, r0 + (16 + 4 * i) * KB) for i in range(2)]
    dh = place("dh", [P, NT, 512], f32r, r0 + 24 * KB)
    dl = place("dl", [P, NT, 512], f32r, r0 + 32 * KB)
    c2s = [place(f"c2s{i}", [P, 2, T], f32, r0 + (40 + 4 * i) * KB) for i in range(2)]
    sls = place("sls", [P, NC, 512], f32, r0 + 48 * KB)
    z = place("z", [P, NT, C], f32, r0 + 52 * KB)
    zh = place("zh", [P, NT, C], f32r, r0 + 56 * KB)
    zl = place("zl", [P, NT, C], f32r, r0 + 60 * KB)
    s1s = place("s1s", [P, NT, E * S], f32, r1)
    xnh = place("xnh", [P, NC, T], f32r, r2)
    xnl = place("xnl", [P, NC, T], f32r, r2 + 4 * KB)
    xn = place("xn", [P, NC, T], f32, r3)
    x1 = place("x1", [P, NT, C], f32, r3 + 4 * KB)
    w3 = place("w3", [P, NC, 3 * C], f32, r0)
    wv = place("wv", [P, NC, C], f32, r0 + 6 * KB)
    wl = place("wl", [P, 2, P], f32, r0 + 8 * KB)
    kvr = place("kvr", [L, P], f32, r0 + 9 * KB)
    l2r = place("l2r", [L, P], f32, r0 + 9 * KB + 512)
    gbd = place("gbd", [P, P], f32, r0 + 10 * KB)
    bvc = place("bvc", [P, NC], f32, r0 + 10 * KB + 512)
    kvb = place("kvb", [L, 1], f32, r0 + 10 * KB + 544)
    bvr = place("bvr", [P, NC, P], f32, r0 + 11 * KB)
    kvbr = place("kvbr", [L, P], f32, r0 + 12 * KB)
    l2b = place("l2b", [1, P], f32, r0 + 12 * KB + 512)
    ones = place("ones", [1, P], f32, r0 + 13 * KB)
    sg = place("sg", [P, NC], f32, r0 + 14 * KB)
    sb_ = place("sb_", [P, NC], f32, r0 + 14 * KB + 32)
    ss = place("ss", [P, 1], f32, r0 + 14 * KB + 64)
    se = place("se", [P, NS, C], f32, r0 + 16 * KB)
    seT = place("seT", [P, NC, E * S], f32, r0 + 24 * KB)
    at[0] = const_end
    eo = place("eo", [P, NS, B, DO], f32)
    p3_start = at[0]
    wg = [place(f"wg{i}", [P, NC, F], f32) for i in range(2)]
    wu = [place(f"wu{i}", [P, NC, F], f32) for i in range(2)]
    wd = [place(f"wd{i}", [P, NF, DO], f32) for i in range(2)]
    wgh, wgl = ([place(f"wg{n}{i}", [P, NC, F], f32r) for i in range(2)] for n in "hl")
    wuh, wul = ([place(f"wu{n}{i}", [P, NC, F], f32r) for i in range(2)] for n in "hl")
    wdh, wdl = ([place(f"wd{n}{i}", [P, NF, DO], f32r) for i in range(2)] for n in "hl")
    sl = [place(f"sl{i}", [P, NC, B * S], f32) for i in range(2)]
    slh = [place(f"slh{i}", [P, NC, B * S], f32r) for i in range(2)]
    sll = [place(f"sll{i}", [P, NC, B * S], f32r) for i in range(2)]
    gate = [place(f"gate{i}", [P, F], f32) for i in range(2)]
    hid = [place(f"hid{i}", [P, B * S], f32) for i in range(2)]
    hh = place("hh", [P, NF, B * S], f32r)
    hl = place("hl", [P, NF, B * S], f32r)
    dt_ = place("dt_", [P, NC, B, 2, S], f32)
    bias_e = [place(f"bias_e{i}", [P, 2 * NF + NC], f32) for i in range(2)]
    at[0] = p3_start
    c2 = place("c2", [P, NS, T], f32)
    c2h = [place(f"c2h{i}", [P, NS, T], f32r) for i in range(2)]
    c2l = [place(f"c2l{i}", [P, NS, T], f32r) for i in range(2)]
    eoh = [place(f"eoh{i}", [P, NS, DO], f32r) for i in range(2)]
    eol = [place(f"eol{i}", [P, NS, DO], f32r) for i in range(2)]
    x1b = [place(f"x1b{i}", [P, NT, C], f32) for i in range(2)]
    y3 = [place(f"y3{i}", [P, NT, C], f32) for i in range(2)]
    st3 = place("st3", [P, NT, 6], f32)
    mv3 = place("mv3", [P, NT, 2], f32)
    v3, r3_, t3 = (place(n, [P, NT], f32) for n in ("v3", "r3_", "t3"))

    ring = [nc.alloc_psum_tensor(f"ring{r}", [P, 2, 512], f32) for r in range(RING)]
    misc = nc.alloc_psum_tensor("misc", [P, 512], f32)
    ybank = nc.alloc_psum_tensor("ybank", [P, 512], f32)

    sem = nc.alloc_semaphore
    loaded = sem("loaded")
    loaded2 = sem("loaded2")
    pool_ready = sem("pool_ready")
    setup_pe = sem("setup_pe")
    setup_dve = sem("setup_dve")
    setup_act = sem("setup_act")
    filled = [sem(f"filled{r}") for r in range(RING)]
    drained = [sem(f"drained{r}") for r in range(RING)]
    misc_filled, misc_drained = sem("misc_filled"), sem("misc_drained")
    y_filled, y_drained = sem("y_filled"), sem("y_drained")
    x_loaded = sem("x_loaded")
    high = sem("high")
    lat_biased = sem("lat_biased")
    shuffled = sem("shuffled")
    sined = sem("sined")
    roped = sem("roped")
    q_high, k_high, k_low = sem("q_high"), sem("k_high"), sem("k_low")
    ones_placed = sem("ones_placed")
    stacked = [sem(f"stacked{g}") for g in range(G)]
    max_placed = [sem(f"max_placed{g}") for g in range(G)]
    neg_ready = sem("neg_ready")
    masked = sem("masked")
    y_normed = sem("y_normed")
    x1_ready, x1_stored = sem("x1_ready"), sem("x1_stored")
    z_ready, z_high, z_low = sem("z_ready"), sem("z_high"), sem("z_low")
    xn_high, xn_low = sem("xn_high"), sem("xn_low")
    s1_max, s2_max = sem("s1_max"), sem("s2_max")
    cs_recip, c1_ready, e2_ready = sem("cs_recip"), sem("c1_ready"), sem("e2_ready")
    c2_stored, sl_stored = [sem(f"c2_stored{i}") for i in range(2)], sem("sl_stored")
    dve_chain = sem("dve_chain")
    waited = sem("waited")
    w_loaded = [sem(f"w_loaded{i}") for i in range(2)]
    w_high, w_low, w_low_pool = sem("w_high"), sem("w_low"), sem("w_low_pool")
    gated, hid_high, hid_low = sem("gated"), sem("hid_high"), sem("hid_low")
    c2_loaded, x1_loaded = sem("c2_loaded"), sem("x1_loaded")
    c2_high, c2_low, eo_high, eo_low = sem("c2_high"), sem("c2_low"), sem("eo_high"), sem("eo_low")
    out_ready, out_stored = sem("out_ready"), sem("out_stored")

    def slot(step):
        return pair_no[step] % RING

    def fill_count(b, step, done=1):
        return b * FILLS[slot(step)] + pair_no[step] // RING + done

    def misc_count(b, step, done=1):
        return b * len(misc_no) + misc_no[step] + done

    def bcast(ap, shape):
        return ap.to_broadcast(shape)

    GBD_DVE, BIAS_DVE, SE_NORM_DVE, SE_DVE, SETUP_DVE = 1, 3, 26, 29, 32
    SETUP_ACT, SETUP_PE = NC, 5
    SETUP_LOADS = 16 * (13 + 3 * (P // HD) + 3 * GH)
    SETUP_LOADS2 = 16 * (2 * (P // HD) + GH + H + 1)
    BATCH_CHAIN, COMBINE_CHAIN = 42, 26
    HIGHS = 1 + 2 * NC + 2 * (NS // 2)

    sin2 = bcast(sin[:, :].unsqueeze(1), [P, 2, T])

    expert_steps = [("gu", 0, f) for f in range(NF)] + [("gu", 1, 0), ("down", 0)]
    expert_steps += [("gu", 1, f) for f in range(1, NF)] + [("down", 1), ("eo", 0), ("eo", 1)]
    EXPERT_FILLS = len(expert_steps) // RING
    expert_no = {s: n for n, s in enumerate(expert_steps)}

    def eslot(step):
        return expert_no[step] % RING

    def ecount(p, step, done=1):
        return B * FILLS[eslot(step)] + p * EXPERT_FILLS + expert_no[step] // RING + done

    def ccount(q, i, done=1):
        return B * FILLS[i] + NP * EXPERT_FILLS + q + done

    def mm3(dst, lh, ll, rh, rl, first, last):
        nc.tensor.matmul(dst, lh, rh, start=first, stop=False)
        nc.tensor.matmul(dst, ll, rh, start=False, stop=False)
        return nc.tensor.matmul(dst, lh, rl, start=False, stop=last)

    def fp(ap):
        return ap.bitcast(f32)

    def apart(engine):
        engine.sem_inc(waited, 1)

    def repeat(engine, round_, n):
        round_(0)
        with engine.Fori(1, n) as i:
            round_(i)

    with nc.Block() as block:

        @block.sync
        def _(sp):
            for dst, src in (
                (w3[:, :, :], a["w_attn_t"].rearrange("(c p) n -> p c n", p=P)),
                (wv[:, :, :], a["c_attn_w"][2 * C:3 * C, :].rearrange("(m p) c -> p m c", p=P)),
                (bqk[:, :], a["b_qk"]),
                (bvc[:, :], a["b_v"]),
                (cos[:, :], a["cos_t"]),
                (sin[:, :], a["sin_t"]),
                (kvb[:, :], a["kv2l_b"].rearrange("(l o) -> l o", o=1)),
                (ng[:, :], a["norm_g"]), (nb_[:, :], a["norm_b"]),
                (sg[:, :], a["slot_g"]), (sb_[:, :], a["slot_b"]),
                (ss[:, :], a["scale"].rearrange("(o n) -> o n", o=1).to_broadcast([P, 1])),
                (se[:, :, :], a["slots"].rearrange("(n p) d -> p n d", p=P)),
            ):
                sp.dma_start(dst, src).then_inc(loaded, 16)
            for h in range(P // HD):
                sp.dma_start(kvr[:, h * HD:(h + 1) * HD], a["kv2l_w"]).then_inc(loaded, 16)
                sp.dma_start(l2r[:, h * HD:(h + 1) * HD], a["l2o_t"]).then_inc(loaded, 16)
                sp.dma_start(l2b[:, h * HD:(h + 1) * HD], a["l2o_b"].rearrange("(o n) -> o n", o=1)).then_inc(loaded, 16)
            for h in range(GH):
                rows = slice(h * L, (h + 1) * L)
                sp.dma_start(blat[rows, 0:1], a["q2l_b"].rearrange("(l o) -> l o", o=1)).then_inc(loaded, 16)
                sp.dma_start(blat[rows, 1:2], a["kv2l_b"].rearrange("(l o) -> l o", o=1)).then_inc(loaded, 16)
                sp.dma_start(bwq[rows, :], a["wqk_b"].rearrange("(l o) -> l o", o=1)).then_inc(loaded, 16)
            sp.wait_ge(pool_ready, 3)
            for h in range(P // HD):
                for w, src in ((0, a["q2l_t"]), (1, a["kv2l_t"])):
                    sp.dma_start(wl[h * HD:(h + 1) * HD, w, h % GH * L:(h % GH + 1) * L], src).then_inc(loaded2, 16)
            for h in range(GH):
                sp.dma_start(wq[h * L:(h + 1) * L, h * L:(h + 1) * L], a["wqk_t"]).then_inc(loaded2, 16)
            for h in range(H):
                sp.dma_start(cw[h % GH * L:h % GH * L + HD, h // GH, :], a["cproj_t"][h * HD:(h + 1) * HD, :]).then_inc(loaded2, 16)
            sp.dma_start(cw[HD:HD + 1, 0, :], a["cproj_b"].rearrange("(o n) -> o n", o=1)).then_inc(loaded2, 16)
            sp.wait_ge(setup_dve, SETUP_DVE)
            sp.wait_ge(setup_act, SETUP_ACT)
            sp.wait_ge(setup_pe, SETUP_PE)

            def batch(b):
                sp.wait_ge(drained[slot(("slots", 1))], b * FILLS[slot(("slots", 1))])
                apart(sp)
                for i in range(2):
                    sp.wait_ge(c2_stored[i], b * 2 * 16)
                    apart(sp)
                sp.wait_ge(sl_stored, b * 2 * NC * 16)
                apart(sp)
                sp.dma_start(fp(qks[KS_ROWS:KS_ROWS + 2, :, :, 1, :]).rearrange("p g h t -> p (g h) t"),
                             bcast(ones2[:, :].unsqueeze(1), [2, H, T])).then_inc(ones_placed, 16)
                for st in steps:
                    if st[0] == "wqk":
                        g, src = st[1], stg[st[1] % 2]
                        sp.wait_ge(misc_drained, misc_count(b, st))
                        apart(sp)
                        sp.wait_ge(k_low, b * G + g + 1)
                        apart(sp)
                        for h in range(GH):
                            rows = slice(h * L, (h + 1) * L)
                            for n, w in enumerate((
                                slice(1, 3),
                                slice(0, 4, 2),
                                slice(1, 4, 2),
                            )):
                                dst, part = qks[n * L:(n + 1) * L, g, h, :, :], src[rows, w, :]
                                sp.dma_start(fp(dst), fp(part)).then_inc(stacked[g], 16)
                    elif st[0] == "negmax":
                        g = st[1]
                        sp.wait_ge(misc_drained, misc_count(b, st))
                        apart(sp)
                        for h in range(GH):
                            sp.dma_start(fp(qks[KS_ROWS:KS_ROWS + 2, g, h, 0, :]),
                                         fp(mts[g % 2][2 * h:2 * h + 2, :])).then_inc(max_placed[g], 16)
                    elif st[0] == "cproj":
                        sp.wait_ge(x1_ready, b + 1)
                        apart(sp)
                        sp.dma_start(x1_dram[b, :, :], x1[:, :, :]).then_inc(x1_stored, 16)
                    elif st[0] == "c2":
                        n = st[1]
                        sp.wait_ge(drained[slot(st)], fill_count(b, st))
                        apart(sp)
                        sp.dma_start(c2_dram[b, :, 2 * n * T:2 * (n + 1) * T], c2s[n % 2][:, :, :]).then_inc(c2_stored[n % 2], 16)
                    elif st[0] == "slots":
                        n = st[1]
                        sp.wait_ge(drained[slot(st)], fill_count(b, st))
                        apart(sp)
                        for d in range(NC):
                            dst = sl_dram[n * (E // 2):(n + 1) * (E // 2), :, d, b, :].rearrange("e p s -> p e s")
                            sp.dma_start(dst, sls[:, d, :].rearrange("p (e s) -> p e s", s=S)).then_inc(sl_stored, 16)

            repeat(sp, batch, B)
            def load_expert(p, i, first=False):
                e = 2 * p + i
                n = bias_e[i]
                if first:
                    sp.wait_ge(sl_stored, B * 2 * NC * 16)
                    for k in range(2):
                        sp.wait_ge(c2_stored[k], B * 2 * 16)
                    sp.wait_ge(x1_stored, B * 16)
                    for r in range(RING):
                        sp.wait_ge(drained[r], B * FILLS[r])
                    sp.wait_ge(y_normed, B * G)
                    sp.wait_ge(c1_ready, B * NT)
                    sp.wait_ge(z_low, B)
                sp.dma_start(sl[i][:, :, :], sl_dram[e, :, :, :, :].rearrange("p c b s -> p c (b s)")).then_inc(w_loaded[i], 16)
                sp.dma_start(wg[i][:, :, :], a["wg"][e, :, :].rearrange("(c p) f -> p c f", p=P)).then_inc(w_loaded[i], 16)
                sp.dma_start(wu[i][:, :, :], a["wu"][e, :, :].rearrange("(c p) f -> p c f", p=P)).then_inc(w_loaded[i], 16)
                sp.dma_start(wd[i][:, :, :], a["wd"][e, :, :].rearrange("(c p) f -> p c f", p=P)).then_inc(w_loaded[i], 16)
                sp.dma_start(n[:, :], a["bias_e"][e, :, :]).then_inc(w_loaded[i], 16)

            load_expert(0, 0, True)
            load_expert(0, 1)
            def pair(p):
                for i in range(2):
                    sp.wait_ge(w_high, (2 * p + i + 1) * 4)
                    apart(sp)
                    sp.wait_ge(w_low, (2 * p + i + 1) * 3)
                    apart(sp)
                    sp.wait_ge(w_low_pool, 2 * p + i + 1)
                    apart(sp)
                    sp.wait_ge(drained[eslot(("down", i))], ecount(p, ("down", i)))
                    apart(sp)
                    load_expert(p + 1, i)

            repeat(sp, pair, NP - 1)
            def load_batch(b, i):
                sp.dma_start(x1b[i][:, :, :], x1_dram[b, :, :]).then_inc(x1_loaded, 16)
                sp.dma_start(c2[:, :, :], c2_dram[b, :, :]).then_inc(c2_loaded, 16)

            sp.wait_ge(drained[eslot(("eo", 1))], ecount(NP - 1, ("eo", 1)))
            def combine(q, i, more):
                b = 2 * q + i
                if more:
                    sp.wait_ge(c2_high, (b + 1) * (NS // 2))
                    apart(sp)
                    sp.wait_ge(c2_low, (b + 1) * (NS // 2))
                    apart(sp)
                    if i == 1:
                        sp.wait_ge(out_ready, b)
                        apart(sp)
                    else:
                        sp.wait_ge(out_ready, 2 * q)
                        apart(sp)
                    load_batch(b + 1, 1 - i)
                sp.wait_ge(out_ready, b + 1)
                apart(sp)
                sp.dma_start(out[b, :, :].rearrange("(n p) c -> p n c", p=P), y3[i][:, :, :]).then_inc(out_stored, 16)

            load_batch(0, 0)
            def combine_two(q):
                for i in range(2):
                    combine(q, i, True)

            repeat(sp, combine_two, B // 2 - 1)
            combine(B // 2 - 1, 0, True)
            combine(B // 2 - 1, 1, False)
            sp.wait_ge(out_stored, B * 16)

        @block.gpsimd
        def _(pool):
            nc.gpsimd.memset(wl[:, :, :], 0.0).then_inc(pool_ready, 1)
            nc.gpsimd.memset(wq[:, :], 0.0).then_inc(pool_ready, 1)
            nc.gpsimd.memset(cw[:, :, :], 0.0).then_inc(pool_ready, 1)
            nc.gpsimd.memset(ident[:, :], 0.0).then_inc(pool_ready, 1)
            nc.gpsimd.memset(identb[:, :], 0.0).then_inc(pool_ready, 1)
            nc.gpsimd.memset(maskb[:, :], 0.0).then_inc(pool_ready, 1)
            nc.gpsimd.memset(pick[:, :], 0.0).then_inc(pool_ready, 1)
            nc.gpsimd.memset(ones[:, :], 1.0).then_inc(pool_ready, 1)
            nc.gpsimd.memset(va[:, :, :, :], 1.0).then_inc(pool_ready, 1)
            nc.gpsimd.memset(ones2[:, :], 1.0).then_inc(pool_ready, 1)
            pool.wait_ge(pool_ready, 10)
            for m in (ident, identb):
                nc.gpsimd.affine_select(out=m[:, :], in_=m[:, :], compare_op=ALU.not_equal, fill=1.0, base=0,
                                        pattern=[[-1, P]], channel_multiplier=1).then_inc(pool_ready, 1)
            nc.gpsimd.affine_select(out=maskb[:, :], in_=maskb[:, :], compare_op=ALU.is_ge, fill=MASKED, base=0,
                                    pattern=[[-1, P]], channel_multiplier=1).then_inc(pool_ready, 1)
            nc.gpsimd.affine_select(out=pick[:, :], in_=pick[:, :], compare_op=ALU.not_equal, fill=1.0, base=-HD,
                                    pattern=[[-L, GH], [0, L]], channel_multiplier=1).then_inc(pool_ready, 1)
            pool.wait_ge(setup_dve, GBD_DVE)
            g3 = gbd[:, :].rearrange("p (h o) -> p h o", o=HD)
            nc.gpsimd.affine_select(out=g3, in_=g3, compare_op=ALU.is_ge, fill=0.0, base=0,
                                    pattern=[[-HD, P // HD], [0, HD]], channel_multiplier=1).then_inc(pool_ready, 1)
            pool.wait_ge(pool_ready, 15)
            nc.gpsimd.affine_select(out=g3, in_=g3, compare_op=ALU.is_ge, fill=0.0, base=HD - 1,
                                    pattern=[[HD, P // HD], [0, HD]], channel_multiplier=-1).then_inc(pool_ready, 1)

            def batch(b):
                last_use = fill_count(b, ("cproj",)) - FILLS[slot(("cproj",))]
                pool.wait_ge(drained[slot(("cproj",))], max(last_use, 0) if isinstance(b, int) else last_use)
                pool.dma_start(x[:, :, :], a["x"][b, :, :].rearrange("(n p) c -> p n c", p=P)).then_inc(x_loaded, 16)
                for st in steps:
                    if st[0] == "wqk":
                        g = st[1]
                        pool.wait_ge(shuffled, b * G + g + 1)
                        nc.gpsimd.tensor_tensor(out=rot[:, :, :], in0=rot[:, :, :], in1=sin2, op=ALU.mult).then_inc(sined, 1)
                        pool.wait_ge(sined, b * G + g + 1)
                        pool.wait_ge(drained[slot(("latent", g))], fill_count(b, ("latent", g)))
                        nc.gpsimd.tensor_tensor(out=rope[:, :, :], in0=rope[:, :, :], in1=rot[:, :, :], op=ALU.add).then_inc(roped, 1)
                        pool.wait_ge(k_high, b * G + g + 1)
                        nc.gpsimd.tensor_tensor(out=stg[g % 2][:, 3, :], in0=rope[:, 1, :], in1=fp(stg[g % 2][:, 2, :]),
                                                op=ALU.subtract).then_inc(k_low, 1)
                    elif st[0] == "exp" and st[3] == 1:
                        g, j = st[1:3]
                        pool.wait_ge(drained[slot(("exp", g, j, 0))], fill_count(b, ("exp", g, j, 0)))
                        pool.wait_ge(drained[slot(st)], fill_count(b, st))
                        apart(pool)
                        m = pt[j % 2][:, :, 0:P]
                        nc.gpsimd.affine_select(out=m, in_=m, compare_op=ALU.is_ge, fill=0.0, base=0,
                                                pattern=[[0, GH], [1, P]], channel_multiplier=-1).then_inc(masked, 1)
                    elif st[0] == "zT":
                        pool.wait_ge(z_high, b + 1)
                        nc.gpsimd.tensor_tensor(out=zl[:, :, :], in0=z[:, :, :], in1=fp(zh[:, :, :]), op=ALU.subtract).then_inc(z_low, 1)
                    elif st[0] == "c1norm":
                        n = st[1]
                        pool.wait_ge(cs_recip, b * NT + n + 1)
                        apart(pool)
                        nc.gpsimd.tensor_scalar(out=c1[:, n, :], in0=c1[:, n, :], scalar1=RCS[:, n:n + 1], scalar2=None,
                                                op0=ALU.mult).then_inc(c1_ready, 1)

            repeat(pool, batch, B)
            def split_low(p, i):
                n = 2 * p + i
                pool.wait_ge(w_high, n * 4 + 3)
                pool.wait_ge(w_loaded[i], (p + 1) * 80)
                nc.gpsimd.tensor_tensor(out=wul[i][:, :, :], in0=wu[i][:, :, :], in1=fp(wuh[i][:, :, :]), op=ALU.subtract).then_inc(w_low_pool, 1)

            def expert(p, i, more):
                if more:
                    split_low(p + i, 1 - i)
                for f in range(NF):
                    n = (2 * p + i) * NF + f
                    pool.wait_ge(hid_high, n + 1)
                    nc.gpsimd.tensor_tensor(out=hl[:, f, :], in0=hid[f % 2][:, :], in1=fp(hh[:, f, :]), op=ALU.subtract).then_inc(hid_low, 1)

            split_low(0, 0)
            def pair(p):
                for i in range(2):
                    expert(p, i, True)

            repeat(pool, pair, NP - 1)
            expert(NP - 1, 0, True)
            expert(NP - 1, 1, False)

            def combine_two(q):
                for i in range(2):
                    b = 2 * q + i
                    pool.wait_ge(eo_high, b + 1)
                    nc.gpsimd.tensor_tensor(out=eol[i][:, :, :], in0=eo[:, :, b, :], in1=fp(eoh[i][:, :, :]), op=ALU.subtract).then_inc(eo_low, 1)

            repeat(pool, combine_two, B // 2)
        @block.scalar
        def _(act):
            for c in range(NC):
                act.wait_ge(setup_dve, SE_DVE + c)
                nc.scalar.activation(seh[:, c, :], seT[:, c, :], ACT.Copy).then_inc(setup_act, 1)

            def batch(b):
                for st in steps:
                    if st[0] in PAIR_STEPS:
                        tile = ring[slot(st)]
                        full, empty = filled[slot(st)], drained[slot(st)]
                    if st[0] == "xT":
                        act.wait_ge(full, fill_count(b, st))
                        nc.scalar.activation(xth[:, :, :], tile[:, :, :], ACT.Copy).then_inc(high, 1)
                    elif st[0] == "qk":
                        act.wait_ge(full, fill_count(b, st))
                        for m in range(NC):
                            n = NC * st[1] + m
                            nc.scalar.activation(qth[:, n, :], tile[:, m, :], ACT.Identity, bias=bqk[:, n:n + 1]).then_inc(high, 1)
                    elif st[0] == "latent":
                        g = st[1]
                        act.wait_ge(full, fill_count(b, st))
                        act.wait_ge(shuffled, b * G + g)
                        if g == 0:
                            act.wait_ge(x1_stored, b * 16)
                        for w in range(2):
                            nc.scalar.activation(lat[:, w, :], tile[:, w, :], ACT.Identity, bias=blat[:, w:w + 1]).then_inc(lat_biased, 1)
                    elif st[0] == "wqk":
                        g = st[1]
                        s = stg[g % 2]
                        act.wait_ge(stacked[(g + 2) % G], (b + (g >= 2)) * 3 * GH * 16)
                        act.wait_ge(roped, b * G + g + 1)
                        nc.scalar.activation(s[:, 2, :], rope[:, 1, :], ACT.Copy).then_inc(k_high, 1)
                        act.wait_ge(misc_filled, misc_count(b, st))
                        nc.scalar.activation(s[:, 1, :], misc[:, :], ACT.Identity, bias=bwq[:, 0:1]).then_inc(q_high, 1)
                    elif st[0] == "negmax":
                        g = st[1]
                        act.wait_ge(misc_filled, misc_count(b, st))
                        act.wait_ge(max_placed[(g + 2) % G], (b + (g >= 2)) * GH * 16)
                        nc.scalar.activation(mts[g % 2][:, :], misc[0:2 * GH, :], ACT.Copy).then_inc(misc_drained, 1)
                    elif st[0] == "exp":
                        g, j, hp = st[1:]
                        n = T - j * P
                        act.wait_ge(full, fill_count(b, st))
                        nc.scalar.activation(pt[j % 2][:, 2 * hp:2 * hp + 2, 0:n], tile[:, :, 0:n], ACT.Exp, scale=SCALE).then_inc(empty, 1)
                    elif st[0] == "y":
                        g = st[1]
                        act.wait_ge(y_filled, b * G + g + 1)
                        act.wait_ge(y_normed, b * G + g)
                        nc.scalar.activation(ys[:, :], ybank[:, :], ACT.Copy).then_inc(y_drained, 1)
                    elif st[0] == "zT":
                        act.wait_ge(z_ready, b + 1)
                        nc.scalar.activation(zh[:, :, :], z[:, :, :], ACT.Copy).then_inc(z_high, 1)
                        act.wait_ge(empty, fill_count(b, st))
                        nc.scalar.activation(xnh[:, :, :], xn[:, :, :], ACT.Copy).then_inc(xn_high, 1)
                    elif st[0] == "s1":
                        n = st[1]
                        act.wait_ge(s1_max, b * NT + n + 1)
                        nc.scalar.activation(s1s[:, n, :].rearrange("p (k s) -> p k s", k=2), tile[:, :, :], ACT.Copy)
                        nc.scalar.activation(c1[:, n, :].rearrange("p (k s) -> p k s", k=2), tile[:, :, :], ACT.Exp,
                                             bias=M1[:, n:n + 1], accum_out=CS[:, n:n + 1]).then_inc(empty, 1)
                    elif st[0] == "s2":
                        n = st[1]
                        act.wait_ge(s2_max, b * (NS // 2) + n + 1)
                        for k in range(2):
                            done = nc.scalar.activation(e2[n % 2][:, k, :], tile[:, k, :], ACT.Exp, bias=M2[:, 2 * n + k:2 * n + k + 1],
                                                        accum_out=ES[:, 2 * n + k:2 * n + k + 1])
                        done.then_inc(empty, 1)
                    elif st[0] == "d":
                        n = st[1]
                        act.wait_ge(full, fill_count(b, st))
                        dst = dh[:, :, n % 2 * 256:n % 2 * 256 + 256].rearrange("p n (k s) -> p k n s", k=2)
                        for k in range(2):
                            nc.scalar.activation(dst[:, k], tile[:, k, :].rearrange("p (n s) -> p n s", n=NT), ACT.Copy).then_inc(high, 1)
                    elif st[0] == "c2":
                        n = st[1]
                        act.wait_ge(full, fill_count(b, st))
                        act.wait_ge(c2_stored[n % 2], (b * 2 + n // 2) * 16)
                        nc.scalar.activation(c2s[n % 2][:, :, :], tile[:, :, :], ACT.Copy).then_inc(empty, 1)
                    elif st[0] == "slots":
                        n = st[1]
                        act.wait_ge(full, fill_count(b, st))
                        act.wait_ge(sl_stored, (b * 2 + n) * NC * 16)
                        for d in range(NC):
                            done = nc.scalar.activation(sls[:, d, :], tile[:, d, :], ACT.Identity, bias=nb_[:, d:d + 1], scale=ng[:, d:d + 1])
                        done.then_inc(empty, 1)

            repeat(act, batch, B)
            raw = [[t[i] for t in (sl, wg, wu, wd)] for i in range(2)]
            highs = [[t[i] for t in (slh, wgh, wuh, wdh)] for i in range(2)]

            def split_high(p, i, k):
                act.wait_ge(w_loaded[i], (p + 1) * 80)
                if k == 0:
                    act.wait_ge(filled[eslot(("down", i))], ecount(p, ("down", i)) - EXPERT_FILLS)
                nc.scalar.activation(highs[i][k][:, :, :], raw[i][k][:, :, :], ACT.Copy).then_inc(w_high, 1)

            def hid_split(p, i, f):
                if f == 0:
                    before = ecount(p, ("down", 0)) if i else ecount(p, ("down", 1)) - EXPERT_FILLS
                    act.wait_ge(filled[eslot(("down", 1 - i))], before)
                act.wait_ge(drained[eslot(("gu", i, f))], ecount(p, ("gu", i, f)))
                nc.scalar.activation(hh[:, f, :], hid[f % 2][:, :], ACT.Copy).then_inc(hid_high, 1)

            def down_bias(p, i):
                st = ("down", i)
                act.wait_ge(filled[eslot(st)], ecount(p, st))
                if i == 0:
                    act.wait_ge(filled[eslot(("eo", 1))], ecount(p, ("eo", 1)) - EXPERT_FILLS)
                for o in range(NC):
                    done = nc.scalar.activation(dt_[:, o, :, i, :], ring[eslot(st)][:, o, :].rearrange("p (b s) -> p b s", b=B),
                                                ACT.Identity, bias=bias_e[i][:, 2 * NF + o:2 * NF + o + 1])
                done.then_inc(drained[eslot(st)], 1)

            def expert(p, i, more):
                for f in range(NF):
                    st = ("gu", i, f)
                    act.wait_ge(filled[eslot(st)], ecount(p, st))
                    nc.scalar.activation(gate[f % 2][:, :], ring[eslot(st)][:, 0, :], ACT.Gelu, bias=bias_e[i][:, f:f + 1]).then_inc(gated, 1)
                    if f:
                        hid_split(p, i, f - 1)
                    elif i == 1:
                        down_bias(p, 0)
                    if more:
                        split_high(p + i, 1 - i, f)
                hid_split(p, i, NF - 1)
                if i == 1:
                    down_bias(p, 1)

            for k in range(4):
                split_high(0, 0, k)
            def pair(p):
                for i in range(2):
                    expert(p, i, True)

            repeat(act, pair, NP - 1)
            expert(NP - 1, 0, True)
            expert(NP - 1, 1, False)

            def combine_two(q):
                for i in range(2):
                    b = 2 * q + i
                    act.wait_ge(filled[i], ccount(q, i, 0))
                    if i == 0:
                        act.wait_ge(drained[eslot(("eo", 1))], ecount(NP - 1, ("eo", 1)))
                        act.wait_ge(drained[eslot(("eo", 0))], ecount(NP - 1, ("eo", 0)))
                    nc.scalar.activation(eoh[i][:, :, :], eo[:, :, b, :], ACT.Copy).then_inc(eo_high, 1)
                    act.wait_ge(c2_loaded, (b + 1) * 16)
                    for k in range(NS // 2):
                        nc.scalar.activation(c2h[i][:, 2 * k:2 * k + 2, :], c2[:, 2 * k:2 * k + 2, :], ACT.Copy).then_inc(c2_high, 1)

            repeat(act, combine_two, B // 2)
        @block.vector
        def _(dve):
            count = [0]

            def link(ins):
                count[0] += 1
                ins.then_inc(setup_dve, 1)
                dve.wait_ge(setup_dve, count[0])

            def rsqrt(link, var, v, y, t):
                link(nc.vector.tensor_scalar(out=v, in0=var, scalar1=EPS, scalar2=None, op0=ALU.add))
                link(nc.vector.tensor_scalar(out=y.bitcast(i32), in0=v.bitcast(i32), scalar1=-0.5, scalar2=RSQRT_MAGIC, op0=ALU.mult, op1=ALU.add))
                for _ in range(NEWTON):
                    link(nc.vector.scalar_tensor_tensor(out=t, in0=y, scalar=-0.5, in1=y, op0=ALU.mult, op1=ALU.mult))
                    link(nc.vector.tensor_tensor(out=t, in0=t, in1=v, op=ALU.mult))
                    link(nc.vector.scalar_tensor_tensor(out=y, in0=t, scalar=1.5, in1=y, op0=ALU.add, op1=ALU.mult))

            dve.wait_ge(loaded, SETUP_LOADS)
            dve.wait_ge(setup_pe, 1)
            link(nc.vector.tensor_copy(gbd[:, :], misc[:, 0:P]))
            assert count[0] == GBD_DVE
            link(nc.vector.tensor_copy(bvr[:, :, :], bcast(bvc[:, :].unsqueeze(2), [P, NC, P])))
            link(nc.vector.tensor_copy(kvbr[:, :], bcast(kvb[:, 0:1], [L, P])))
            assert count[0] == BIAS_DVE
            for c in range(NC):
                link(nc.vector.tensor_copy(w3h[:, c, 0:2 * C], w3[:, c, 0:2 * C]))
                link(nc.vector.tensor_tensor(out=w3l[:, c, 0:2 * C], in0=w3[:, c, 0:2 * C], in1=fp(w3h[:, c, 0:2 * C]), op=ALU.subtract))
            dve.wait_ge(loaded2, SETUP_LOADS2)
            link(nc.vector.tensor_copy(wlh[:, :, :], wl[:, :, :]))
            link(nc.vector.tensor_tensor(out=wll[:, :, :], in0=wl[:, :, :], in1=fp(wlh[:, :, :]), op=ALU.subtract))
            dve.wait_ge(setup_pe, 2)
            link(nc.vector.tensor_copy(w3h[:, :, 2 * C:3 * C], ring[0][:, :, 0:C]))
            link(nc.vector.tensor_tensor(out=w3l[:, :, 2 * C:3 * C], in0=ring[0][:, :, 0:C], in1=fp(w3h[:, :, 2 * C:3 * C]), op=ALU.subtract))
            dve.wait_ge(setup_pe, 3)
            link(nc.vector.tensor_copy(bv[:, :], ring[1][:, 0, 0:C]))
            for n in range(NS):
                last = nc.vector.bn_stats(stats[:, n, :], se[:, n, :])
            link(last)
            for n in range(NS):
                last = nc.vector.bn_aggr(meanvar[:, n, :], stats[:, n, :])
            link(last)
            rsqrt(link, meanvar[:, :, 1], nv[:, :], ny[:, :], nt_[:, :])
            for n in range(NS):
                last = nc.vector.tensor_scalar(out=se[:, n, :], in0=se[:, n, :], scalar1=meanvar[:, n, 0:1], scalar2=ny[:, n:n + 1],
                                               op0=ALU.subtract, op1=ALU.mult)
            link(last)
            assert count[0] == SE_NORM_DVE
            link(nc.vector.tensor_scalar(out=sg[:, :], in0=sg[:, :], scalar1=ss[:, 0:1], scalar2=None, op0=ALU.mult))
            link(nc.vector.tensor_scalar(out=sb_[:, :], in0=sb_[:, :], scalar1=ss[:, 0:1], scalar2=None, op0=ALU.mult))
            for c in range(NC):
                dve.wait_ge(setup_pe, 4 + c)
                src = (ring[2], ring[0])[c]
                link(nc.vector.tensor_scalar(out=seT[:, c, :].rearrange("p (k s) -> p k s", k=2), in0=src[:, :, :],
                                             scalar1=sg[:, c:c + 1], scalar2=sb_[:, c:c + 1], op0=ALU.mult, op1=ALU.add))
                assert count[0] == SE_DVE + c
            for c in range(NC):
                dve.wait_ge(setup_act, c + 1)
                link(nc.vector.tensor_tensor(out=sel_[:, c, :], in0=seT[:, c, :], in1=fp(seh[:, c, :]), op=ALU.subtract))
            assert count[0] == SETUP_DVE, count[0]

            def batch(b):
                chain = [0]

                def blink(ins):
                    chain[0] += 1
                    ins.then_inc(dve_chain, 1)
                    dve.wait_ge(dve_chain, b * BATCH_CHAIN + chain[0])
                    apart(dve)

                def norm(src, dst, nmean, n):
                    for k in range(n):
                        last = nc.vector.bn_stats(stats[:, k, :], src[:, k, :])
                    blink(last)
                    for k in range(n):
                        last = nc.vector.bn_aggr(meanvar[:, k, :], stats[:, k, :])
                    blink(last)
                    rsqrt(blink, meanvar[:, 0:n, 1], nv[:, 0:n], ny[:, 0:n], nt_[:, 0:n])
                    for k in range(n):
                        last = nc.vector.tensor_scalar(out=dst[:, k, :], in0=src[:, k, :], scalar1=meanvar[:, k, 0:1],
                                                       scalar2=ny[:, k:k + 1], op0=ALU.subtract, op1=ALU.mult)
                    return last

                for st in steps:
                    if st[0] in PAIR_STEPS:
                        tile = ring[slot(st)]
                        full, empty = filled[slot(st)], drained[slot(st)]
                    if st[0] == "xT":
                        dve.wait_ge(high, b * HIGHS + 1)
                        nc.vector.tensor_tensor(out=xtl[:, :, :], in0=tile[:, :, :], in1=fp(xth[:, :, :]), op=ALU.subtract).then_inc(empty, 1)
                    elif st[0] == "qk":
                        dve.wait_ge(high, b * HIGHS + 1 + NC * (st[1] + 1))
                        for m in range(NC):
                            n = NC * st[1] + m
                            last = nc.vector.scalar_tensor_tensor(out=qtl[:, n, :], in0=tile[:, m, :], scalar=bqk[:, n:n + 1],
                                                                  in1=fp(qth[:, n, :]), op0=ALU.add, op1=ALU.subtract)
                        last.then_inc(empty, 1)
                    elif st[0] == "v":
                        dve.wait_ge(full, fill_count(b, st))
                        for k in range(2):
                            last = nc.vector.tensor_tensor(
                                out=va[:, 2 * k:2 * k + 2, :, 0:HD],
                                in0=tile[:, k, :].rearrange("p (t h o) -> p t h o", t=2, o=HD),
                                in1=bcast(bv[:, :].rearrange("p (h o) -> p h o", o=HD).unsqueeze(1), [P, 2, H, HD]), op=ALU.add)
                        last.then_inc(empty, 1)
                    elif st[0] == "latent":
                        g = st[1]
                        dve.wait_ge(lat_biased, (b * G + g + 1) * 2)
                        dve.wait_ge(roped, b * G + g)
                        apart(dve)
                        nc.vector.stream_shuffle(rot[:, :, :], lat[:, :, :], [i ^ 1 for i in range(L)]).then_inc(shuffled, 1)
                        dve.wait_ge(k_low, b * G + g)
                        if g:
                            dve.wait_ge(misc_filled, misc_count(b, ("wqk", g - 1)))
                        for w in range(2):
                            last = nc.vector.scalar_tensor_tensor(out=rope[:, w, :], in0=tile[:, w, :], scalar=blat[:, w:w + 1],
                                                                  in1=cos[:, :], op0=ALU.add, op1=ALU.mult)
                        last.then_inc(empty, 1)
                    elif st[0] == "wqk":
                        g = st[1]
                        dve.wait_ge(q_high, b * G + g + 1)
                        nc.vector.scalar_tensor_tensor(out=stg[g % 2][:, 0, :], in0=misc[:, :], scalar=bwq[:, 0:1],
                                                       in1=fp(stg[g % 2][:, 1, :]), op0=ALU.add, op1=ALU.subtract).then_inc(misc_drained, 1)
                    elif st[0] == "max":
                        g, i, hp = st[1:]
                        dve.wait_ge(full, fill_count(b, st))
                        nc.vector.tensor_reduce(out=mx[:, g, i, 2 * hp:2 * hp + 2], in_=tile[:, :, 0:(i + 1) * P], axis=AX.X,
                                                op=ALU.max).then_inc(empty, 1)
                    elif st[0] == "negmax":
                        g = st[1]
                        dve.wait_ge(drained[slot(("max", g, NT - 1, 1))], fill_count(b, ("max", g, NT - 1, 1)))
                        dve.wait_ge(drained[slot(("max", g, NT - 1, 0))], fill_count(b, ("max", g, NT - 1, 0)))
                        dve.wait_ge(drained[slot(("max", g, NT - 2, 1))], fill_count(b, ("max", g, NT - 2, 1)))
                        blink(nc.vector.tensor_scalar(out=negmax[:, g, :, :, 0].bitcast(f32r), in0=mx[:, g, :, :], scalar1=-1.0,
                                                      scalar2=None, op0=ALU.mult))
                        nc.vector.scalar_tensor_tensor(out=negmax[:, g, :, :, 1].bitcast(f32r), in0=mx[:, g, :, :], scalar=-1.0,
                                                       in1=negmax[:, g, :, :, 0], op0=ALU.mult, op1=ALU.subtract).then_inc(neg_ready, 1)
                    elif st[0] == "ynorm":
                        g = st[1]
                        dve.wait_ge(misc_filled, misc_count(b, st))
                        nc.vector.reciprocal(rc[:, :], misc[:, :]).then_inc(misc_drained, 1)
                        dve.wait_ge(misc_drained, misc_count(b, st))
                        nc.vector.tensor_tensor(out=yn[:, g, :], in0=ys[:, :], in1=rc[:, :], op=ALU.mult).then_inc(y_normed, 1)
                    elif st[0] == "cproj":
                        dve.wait_ge(full, fill_count(b, st))
                        nc.vector.tensor_tensor(out=x1[:, :, :].rearrange("p (k t) c -> p k (t c)", k=2), in0=tile[:, :, :],
                                                in1=x[:, :, :].rearrange("p (k t) c -> p k (t c)", k=2), op=ALU.add).then_inc(empty, 1)
                        dve.wait_ge(empty, fill_count(b, st))
                        norm(x1, x1, 0, NT).then_inc(x1_ready, 1)
                        dve.wait_ge(x1_ready, b + 1)
                        norm(x1, z, 0, NT).then_inc(z_ready, 1)
                    elif st[0] == "zT":
                        dve.wait_ge(full, fill_count(b, st))
                        for c in range(NC):
                            last = nc.vector.tensor_scalar(out=xn[:, c, :], in0=tile[:, c, :], scalar1=ng[:, c:c + 1], scalar2=nb_[:, c:c + 1],
                                                           op0=ALU.mult, op1=ALU.add)
                        last.then_inc(empty, 1)
                        dve.wait_ge(xn_high, b + 1)
                        nc.vector.tensor_tensor(out=xnl[:, :, :], in0=xn[:, :, :], in1=fp(xnh[:, :, :]), op=ALU.subtract).then_inc(xn_low, 1)
                    elif st[0] == "s1":
                        n = st[1]
                        dve.wait_ge(full, fill_count(b, st))
                        blink(nc.vector.tensor_reduce(out=M1[:, n:n + 1], in_=tile[:, :, :], axis=AX.XY, op=ALU.max))
                        nc.vector.tensor_scalar(out=M1[:, n:n + 1], in0=M1[:, n:n + 1], scalar1=-1.0, scalar2=None, op0=ALU.mult).then_inc(s1_max, 1)
                    elif st[0] == "c1norm":
                        n = st[1]
                        src = ("s1", n)
                        dve.wait_ge(drained[slot(src)], fill_count(b, src))
                        nc.vector.reciprocal(RCS[:, n:n + 1], CS[:, n:n + 1]).then_inc(cs_recip, 1)
                    elif st[0] == "s2":
                        n = st[1]
                        dve.wait_ge(full, fill_count(b, st))
                        m = M2[:, 2 * n:2 * n + 2]
                        blink(nc.vector.tensor_reduce(out=m, in_=tile[:, :, :], axis=AX.X, op=ALU.max))
                        nc.vector.tensor_scalar(out=m, in0=m, scalar1=-1.0, scalar2=None, op0=ALU.mult).then_inc(s2_max, 1)
                    elif st[0] == "e2norm":
                        n = st[1]
                        src = ("s2", n)
                        dve.wait_ge(drained[slot(src)], fill_count(b, src))
                        blink(nc.vector.reciprocal(RES[:, 2 * n:2 * n + 2], ES[:, 2 * n:2 * n + 2]))
                        for k in range(2):
                            last = nc.vector.tensor_scalar(out=e2[n % 2][:, k, :], in0=e2[n % 2][:, k, :], scalar1=RES[:, 2 * n + k:2 * n + k + 1],
                                                           scalar2=None, op0=ALU.mult)
                        last.then_inc(e2_ready, 1)
                    elif st[0] == "d":
                        n = st[1]
                        dve.wait_ge(high, b * HIGHS + 1 + 2 * NC + 2 * (n + 1))
                        cols = slice(n % 2 * 256, n % 2 * 256 + 256)
                        for k in range(2):
                            last = nc.vector.tensor_tensor(out=dl[:, :, cols].rearrange("p n (k s) -> p k n s", k=2)[:, k],
                                                           in0=tile[:, k, :].rearrange("p (n s) -> p n s", n=NT),
                                                           in1=fp(dh[:, :, cols]).rearrange("p n (k s) -> p k n s", k=2)[:, k], op=ALU.subtract)
                        last.then_inc(empty, 1)
                assert chain[0] == BATCH_CHAIN, chain[0]

            repeat(dve, batch, B)

            raw = [[t[i] for t in (sl, wg, wu, wd)] for i in range(2)]
            highs = [[t[i] for t in (slh, wgh, wuh, wdh)] for i in range(2)]
            lows = [[t[i] for t in (sll, wgl, wul, wdl)] for i in range(2)]

            def split_low(p, i, k):
                dve.wait_ge(w_high, (2 * p + i) * 4 + k + 1)
                nc.vector.tensor_tensor(out=lows[i][k][:, :, :], in0=raw[i][k][:, :, :], in1=fp(highs[i][k][:, :, :]),
                                        op=ALU.subtract).then_inc(w_low, 1)

            def expert(p, i, more):
                for f in range(NF):
                    st = ("gu", i, f)
                    n = (2 * p + i) * NF
                    dve.wait_ge(gated, n + f + 1)
                    dve.wait_ge(hid_low, n + max(f - 1, 0))
                    nc.vector.scalar_tensor_tensor(out=hid[f % 2][:, :], in0=ring[eslot(st)][:, 1, :], scalar=bias_e[i][:, NF + f:NF + f + 1],
                                                   in1=gate[f % 2][:, :], op0=ALU.add, op1=ALU.mult).then_inc(drained[eslot(st)], 1)
                    if more and f != 2:
                        split_low(p + i, 1 - i, f)
                if i == 1:
                    for k in range(2):
                        st = ("eo", k)
                        dve.wait_ge(filled[eslot(st)], ecount(p, st))
                        nc.vector.tensor_copy(eo[:, p, 4 * k:4 * k + 4, :].rearrange("p (k b) o -> p k (b o)", k=2),
                                              ring[eslot(st)][:, :, :]).then_inc(drained[eslot(st)], 1)

            for k in (0, 1, 3):
                split_low(0, 0, k)
            def pair(p):
                for i in range(2):
                    expert(p, i, True)

            repeat(dve, pair, NP - 1)
            expert(NP - 1, 0, True)
            expert(NP - 1, 1, False)

            def combine_two(q):
                chain = [0]

                def clink(ins):
                    chain[0] += 1
                    ins.then_inc(dve_chain, 1)
                    dve.wait_ge(dve_chain, B * BATCH_CHAIN + q * COMBINE_CHAIN + chain[0])
                    apart(dve)

                for i in range(2):
                    b = 2 * q + i
                    for k in range(NS // 2):
                        dve.wait_ge(c2_high, b * (NS // 2) + k + 1)
                        nc.vector.tensor_tensor(out=c2l[i][:, 2 * k:2 * k + 2, :], in0=c2[:, 2 * k:2 * k + 2, :],
                                                in1=fp(c2h[i][:, 2 * k:2 * k + 2, :]), op=ALU.subtract).then_inc(c2_low, 1)
                    dve.wait_ge(filled[i], ccount(q, i))
                    dve.wait_ge(x1_loaded, (b + 1) * 16)
                    dve.wait_ge(out_stored, 2 * q * 16)
                    y = y3[i]
                    nc.vector.tensor_tensor(out=y[:, :, :].rearrange("p (k t) c -> p k (t c)", k=2), in0=ring[i][:, :, :],
                                            in1=x1b[i][:, :, :].rearrange("p (k t) c -> p k (t c)", k=2), op=ALU.add).then_inc(drained[i], 1)
                    dve.wait_ge(drained[i], ccount(q, i))
                    for k in range(NT):
                        last = nc.vector.bn_stats(st3[:, k, :], y[:, k, :])
                    clink(last)
                    for k in range(NT):
                        last = nc.vector.bn_aggr(mv3[:, k, :], st3[:, k, :])
                    clink(last)
                    rsqrt(clink, mv3[:, :, 1], v3[:, :], r3_[:, :], t3[:, :])
                    for k in range(NT):
                        last = nc.vector.tensor_scalar(out=y[:, k, :], in0=y[:, k, :], scalar1=mv3[:, k, 0:1], scalar2=r3_[:, k:k + 1],
                                                       op0=ALU.subtract, op1=ALU.mult)
                    last.then_inc(out_ready, 1)
                assert chain[0] == COMBINE_CHAIN, chain[0]

            repeat(dve, combine_two, B // 2)

        @block.tensor
        def _(pe):
            pe.wait_ge(loaded, SETUP_LOADS)
            nc.tensor.matmul(misc[:, 0:P], kvr[:, :], l2r[:, :], start=True, stop=True).then_inc(setup_pe, 1)
            pe.wait_ge(pool_ready, 16)
            for c in range(NC):
                for m in range(NC):
                    last = nc.tensor.matmul(ring[0][:, c, m * P:(m + 1) * P], wv[:, m, c * P:(c + 1) * P], gbd[:, :], start=True, stop=True)
            last.then_inc(setup_pe, 1)
            pe.wait_ge(setup_dve, BIAS_DVE)
            for m in range(NC):
                dst = ring[1][:, 0, m * P:(m + 1) * P]
                nc.tensor.matmul(dst, bvr[:, m, :], gbd[:, :], start=True, stop=False)
                nc.tensor.matmul(dst, kvbr[:, :], l2r[:, :], start=False, stop=False)
                last = nc.tensor.matmul(dst, ones[:, :], l2b[:, :], start=False, stop=True)
            last.then_inc(setup_pe, 1)
            pe.wait_ge(setup_dve, SE_NORM_DVE)
            for c in range(NC):
                for n in range(NS):
                    last = nc.tensor.transpose((ring[2], ring[0])[c][:, n // 4, n % 4 * P:(n % 4 + 1) * P], se[:, n, c * P:(c + 1) * P], ident[:, :])
                last.then_inc(setup_pe, 1)
            pe.wait_ge(setup_dve, SETUP_DVE)
            pe.wait_ge(loaded2, SETUP_LOADS2)

            def batch(b):
                for st in steps:
                    if st[0] in PAIR_STEPS:
                        tile = ring[slot(st)]
                        full, empty = filled[slot(st)], drained[slot(st)]
                        pe.wait_ge(empty, fill_count(b, st, 0))
                    elif st[0] in MISC_STEPS:
                        pe.wait_ge(misc_drained, misc_count(b, st, 0))

                    def ready(src):
                        pe.wait_ge(drained[slot(src)], fill_count(b, src))

                    if st[0] == "xT":
                        pe.wait_ge(x_loaded, (b + 1) * 16)
                        for c in range(NC):
                            for t in range(NT):
                                last = nc.tensor.transpose(tile[:, c, t * P:(t + 1) * P], x[:, t, c * P:(c + 1) * P], ident[:, :])
                        last.then_inc(full, 1)
                    elif st[0] == "qk":
                        if st[1] == 0:
                            ready(("xT",))
                        for m in range(NC):
                            cols = slice(st[1] * C + m * P, st[1] * C + (m + 1) * P)
                            for c in range(NC):
                                last = mm3(tile[:, m, :], w3h[:, c, cols], w3l[:, c, cols], xth[:, c, :], xtl[:, c, :], c == 0, c == NC - 1)
                        last.then_inc(full, 1)
                    elif st[0] == "v":
                        for t in range(NT):
                            rows = slice(t * P, (t + 1) * P)
                            for c in range(NC):
                                last = mm3(tile[:, t // 2, t % 2 * C:(t % 2 + 1) * C], xth[:, c, rows], xtl[:, c, rows],
                                           w3h[:, c, 2 * C:3 * C], w3l[:, c, 2 * C:3 * C], c == 0, c == NC - 1)
                        last.then_inc(full, 1)
                    elif st[0] == "latent":
                        g = st[1]
                        if g == 0:
                            ready(("qk", 0))
                            ready(("qk", 1))
                        rows = slice(g % 2 * 64, g % 2 * 64 + 64)
                        for w in range(2):
                            n = NC * w + g // 2
                            last = mm3(tile[:, w, :], wlh[rows, w, :], wll[rows, w, :], qth[rows, n, :], qtl[rows, n, :], True, True)
                        last.then_inc(full, 1)
                    elif st[0] == "wqk":
                        pe.wait_ge(roped, b * G + st[1] + 1)
                        nc.tensor.matmul(misc[:, :], wq[:, :], rope[:, 0, :], start=True, stop=True).then_inc(misc_filled, 1)
                    elif st[0] == "max":
                        g, i, hp = st[1:]
                        if (i, hp) == (0, 0):
                            pe.wait_ge(stacked[g], (b + 1) * 3 * GH * 16)
                        for k in range(2):
                            h = 2 * hp + k
                            nc.tensor.matmul(tile[:, k, 0:(i + 1) * P], qks[0:KS_ROWS, g, h, 0, i * P:(i + 1) * P],
                                             qks[0:KS_ROWS, g, h, 1, 0:(i + 1) * P], start=True, stop=False)
                            last = nc.tensor.matmul(tile[:, k, i * P:(i + 1) * P], identb[:, :], maskb[:, :], start=False, stop=True)
                        last.then_inc(full, 1)
                    elif st[0] == "negmax":
                        g = st[1]
                        pe.wait_ge(neg_ready, b * G + g + 1)
                        for i in range(NT):
                            last = nc.tensor.transpose(misc[0:2 * GH, i * P:(i + 1) * P], negmax[:, g, i, :, :].rearrange("p h k -> p (h k)"), ident[:, :])
                        last.then_inc(misc_filled, 1)
                    elif st[0] == "exp":
                        g, j, hp = st[1:]
                        if (j, hp) == (0, 0):
                            pe.wait_ge(max_placed[g], (b + 1) * GH * 16)
                            pe.wait_ge(ones_placed, (b + 1) * 16)
                        for k in range(2):
                            h = 2 * hp + k
                            last = nc.tensor.matmul(tile[:, k, 0:T - j * P], qks[0:KS_ROWS + 2, g, h, 1, j * P:(j + 1) * P],
                                                    qks[0:KS_ROWS + 2, g, h, 0, j * P:T], start=True, stop=True)
                        last.then_inc(full, 1)
                    elif st[0] == "pv":
                        g, j = st[1:]
                        pe.wait_ge(masked, (b * G + g) * NT + j + 1)
                        if j == 0:
                            pe.wait_ge(y_drained, b * G + g)
                        for h in range(GH):
                            last = nc.tensor.matmul(ybank[h * L:(h + 1) * L, j * P:T], va[:, j, g * GH + h, :], pt[j % 2][:, h, 0:T - j * P],
                                                    start=(j == 0), stop=(j == NT - 1))
                        if j == NT - 1:
                            last.then_inc(y_filled, 1)
                    elif st[0] == "ynorm":
                        g = st[1]
                        pe.wait_ge(y_drained, b * G + g + 1)
                        nc.tensor.matmul(misc[:, :], pick[:, :], ys[:, :], start=True, stop=True).then_inc(misc_filled, 1)
                    elif st[0] == "cproj":
                        pe.wait_ge(y_normed, (b + 1) * G)
                        for t in range(NT):
                            for g in range(G):
                                last = nc.tensor.matmul(tile[:, t // 2, t % 2 * C:(t % 2 + 1) * C], yn[:, g, t * P:(t + 1) * P], cw[:, g, :],
                                                        start=(g == 0), stop=(g == G - 1))
                        last.then_inc(full, 1)
                    elif st[0] == "zT":
                        pe.wait_ge(z_ready, b + 1)
                        for c in range(NC):
                            for t in range(NT):
                                last = nc.tensor.transpose(tile[:, c, t * P:(t + 1) * P], z[:, t, c * P:(c + 1) * P], ident[:, :])
                        last.then_inc(full, 1)
                    elif st[0] == "s1":
                        t = st[1]
                        if t == 0:
                            pe.wait_ge(xn_low, b + 1)
                        rows = slice(t * P, (t + 1) * P)
                        for k in range(2):
                            cols = slice(k * 512, (k + 1) * 512)
                            for c in range(NC):
                                last = mm3(tile[:, k, :], xnh[:, c, rows], xnl[:, c, rows], seh[:, c, cols], sel_[:, c, cols], c == 0, c == NC - 1)
                        last.then_inc(full, 1)
                    elif st[0] == "s2":
                        n = st[1]
                        if n == 0:
                            for t in range(NT):
                                ready(("s1", t))
                        for k in range(2):
                            for t in range(NT):
                                last = nc.tensor.transpose(tile[:, k, t * P:(t + 1) * P], s1s[:, t, (2 * n + k) * P:(2 * n + k + 1) * P], ident[:, :])
                        last.then_inc(full, 1)
                    elif st[0] == "d":
                        n = st[1]
                        pe.wait_ge(e2_ready, b * (NS // 2) + n + 1)
                        for k in range(2):
                            for t in range(NT):
                                last = nc.tensor.transpose(tile[:, k, t * P:(t + 1) * P], e2[n % 2][:, k, t * P:(t + 1) * P], ident[:, :])
                        last.then_inc(full, 1)
                    elif st[0] == "c2":
                        n = st[1]
                        if n == 0:
                            pe.wait_ge(c1_ready, (b + 1) * NT)
                        for k in range(2):
                            for t in range(NT):
                                last = nc.tensor.transpose(tile[:, k, t * P:(t + 1) * P], c1[:, t, (2 * n + k) * P:(2 * n + k + 1) * P], ident[:, :])
                        last.then_inc(full, 1)
                    elif st[0] == "slots":
                        n = st[1]
                        ready(("d", 2 * n))
                        ready(("d", 2 * n + 1))
                        if n == 0:
                            pe.wait_ge(z_low, b + 1)
                        for d in range(NC):
                            for t in range(NT):
                                last = mm3(tile[:, d, :], zh[:, t, d * P:(d + 1) * P], zl[:, t, d * P:(d + 1) * P], dh[:, t, :], dl[:, t, :],
                                           t == 0, t == NT - 1)
                        last.then_inc(full, 1)

            repeat(pe, batch, B)
            def expert_step(p, st):
                tile = ring[eslot(st)]
                pe.wait_ge(drained[eslot(st)], ecount(p, st, 0))
                if st[0] == "gu":
                    i, f = st[1:]
                    if f == 0:
                        pe.wait_ge(w_low, (2 * p + i + 1) * 3)
                        pe.wait_ge(w_low_pool, 2 * p + i + 1)
                    cols = slice(f * P, (f + 1) * P)
                    for k, (wh, wlo) in enumerate(((wgh[i], wgl[i]), (wuh[i], wul[i]))):
                        for c in range(NC):
                            last = mm3(tile[:, k, :], wh[:, c, cols], wlo[:, c, cols], slh[i][:, c, :], sll[i][:, c, :], c == 0, c == NC - 1)
                elif st[0] == "down":
                    i = st[1]
                    pe.wait_ge(hid_low, (2 * p + i + 1) * NF)
                    for o in range(NC):
                        cols = slice(o * P, (o + 1) * P)
                        for f in range(NF):
                            last = mm3(tile[:, o, :], wdh[i][:, f, cols], wdl[i][:, f, cols], hh[:, f, :], hl[:, f, :], f == 0, f == NF - 1)
                else:
                    k = st[1]
                    if k == 0:
                        for i in range(2):
                            pe.wait_ge(drained[eslot(("down", i))], ecount(p, ("down", i)))
                    for n in range(4):
                        for o in range(NC):
                            last = nc.tensor.transpose(tile[:, n // 2, n % 2 * DO + o * P:n % 2 * DO + (o + 1) * P],
                                                       dt_[:, o, 4 * k + n, :, :].rearrange("p e s -> p (e s)"), ident[:, :])
                last.then_inc(filled[eslot(st)], 1)

            def pair(p):
                for st in expert_steps:
                    expert_step(p, st)

            repeat(pe, pair, NP)
            def combine_two(q):
                for i in range(2):
                    b = 2 * q + i
                    pe.wait_ge(drained[i], ccount(q, i, 0))
                    pe.wait_ge(c2_low, (b + 1) * (NS // 2))
                    pe.wait_ge(eo_low, b + 1)
                    for t in range(NT):
                        rows = slice(t * P, (t + 1) * P)
                        for n in range(NS):
                            last = mm3(ring[i][:, t // 2, t % 2 * DO:(t % 2 + 1) * DO], c2h[i][:, n, rows], c2l[i][:, n, rows],
                                       eoh[i][:, n, :], eol[i][:, n, :], n == 0, n == NS - 1)
                    last.then_inc(filled[i], 1)

            repeat(pe, combine_two, B // 2)
def kernel(**inputs):
    import numpy as np
    import concourse.bacc as bacc
    from concourse.bass_utils import run_bass_kernel_spmd

    def blocks(v):
        return np.ascontiguousarray(v.reshape(-1, P).T)

    n = {k.replace("L0_attn_", "").replace("L0_ffn_", ""): np.asarray(v) for k, v in inputs.items()}
    freq = np.float32(1.0) / np.float32(10000.0) ** (np.arange(0, L, 2, dtype=np.float32) / np.float32(L))
    angle = np.repeat(np.outer(np.arange(T, dtype=np.float32), freq), 2, axis=1).T
    sign = np.where(np.arange(L) % 2 == 0, np.float32(-1.0), np.float32(1.0))[:, None]
    arrays = {
        "x": n["x"], "c_attn_w": n["c_attn_w"], "w_attn_t": n["c_attn_w"].T,
        "b_qk": blocks(n["c_attn_b"][0:2 * C]), "b_v": blocks(n["c_attn_b"][2 * C:3 * C]),
        "cos_t": np.tile(np.cos(angle), (GH, 1)), "sin_t": np.tile(np.sin(angle) * sign, (GH, 1)),
        "q2l_t": n["q2l_w"].T, "q2l_b": n["q2l_b"], "kv2l_w": n["kv2l_w"], "kv2l_t": n["kv2l_w"].T, "kv2l_b": n["kv2l_b"],
        "l2o_t": n["l2o_w"].T, "l2o_b": n["l2o_b"], "wqk_t": n["wqk_w"].T, "wqk_b": n["wqk_b"],
        "cproj_t": n["cproj_w"].T, "cproj_b": n["cproj_b"],
        "norm_g": blocks(n["norm_g"]), "norm_b": blocks(n["norm_b"]), "slot_g": blocks(n["slot_g"]), "slot_b": blocks(n["slot_b"]),
        "scale": n["scale"], "slots": n["slot_embeds"].reshape(E * S, C), "wg": n["Wg"], "wu": n["Wu"], "wd": n["Wd"],
        "bias_e": np.concatenate([n["bg"].reshape(E, NF, P), n["bu"].reshape(E, NF, P), n["bd"].reshape(E, NC, P)], axis=1).transpose(0, 2, 1),
    }
    arrays = {k: np.ascontiguousarray(v) for k, v in arrays.items()}
    nc = bacc.Bacc("TRN2", target_bir_lowering=False, num_devices=1)
    aps = {k: nc.dram_tensor(f"in_{k}", v.shape, mybir.dt.from_np(v.dtype), kind="ExternalInput").ap() for k, v in arrays.items()}
    out = nc.dram_tensor("out", (B, T, C), mybir.dt.float32, kind="ExternalOutput").ap()
    block_kernel(nc, aps, out)
    r = run_bass_kernel_spmd(nc, [{f"in_{k}": v for k, v in arrays.items()}], core_ids=[0])
    return r.results[0]["out"]
```
